# Optimizing a Trainium2 kernel written in Bass

```python
import numpy as np
import jax
import jax.numpy as jnp

def _softmax(x, axis=-1):
    return jax.nn.softmax(x, axis=axis)

def _gelu(x):
    return jax.nn.gelu(x, approximate=True)

def _silu(x):
    return jax.nn.silu(x)

def _sigmoid(x):
    return jax.nn.sigmoid(x)

def _layernorm(x, axis=-1, eps=1e-05):
    m = jnp.mean(x, axis=axis, keepdims=True)
    v = jnp.var(x, axis=axis, keepdims=True)
    return (x - m) / jnp.sqrt(v + eps)

def _scatter_add(tgt, idx, src, axis=0):
    return tgt.at[idx].add(src)

def _segment_sum(src, seg, n):
    return jax.ops.segment_sum(src, seg, n)
kernel_name = 'mk_seq_preln_d2_jaxref_r4_5d5b9b'

def setup_inputs(seed: int=0):
    np.random.seed(seed)
    _w = jnp.asarray

    def _L0_attn_setup():
        import jax, jax.numpy as jnp
        import numpy as np
        EMB = 256
        HEADS = 16
        WINDOW = 128
        key = jax.random.key(seed)
        ks = jax.random.split(key, 9)
        B, N = (2, 512)
        s = 0.02
        f32 = jnp.float32
        return {'x': jax.random.normal(ks[0], (B, N, EMB), dtype=f32), 'Wq': jax.random.normal(ks[1], (EMB, EMB), dtype=f32) * s, 'bq': jnp.zeros((EMB,), dtype=f32), 'Wk': jax.random.normal(ks[2], (EMB, EMB), dtype=f32) * s, 'bk': jnp.zeros((EMB,), dtype=f32), 'Wv': jax.random.normal(ks[3], (EMB, EMB), dtype=f32) * s, 'bv': jnp.zeros((EMB,), dtype=f32), 'Wp': jax.random.normal(ks[4], (EMB, EMB), dtype=f32) * s, 'bp': jnp.zeros((EMB,), dtype=f32)}
    _L0_attn_in = _L0_attn_setup()

    def _L0_ffn_setup():
        import jax, jax.numpy as jnp
        import numpy as np
        B, T, D = (4, 1024, 256)
        E = 8
        TOP_K = 2
        FFN = 768
        HALF = FFN // 2

        def _kaiming_uniform(key, shape, fan_in):
            bound = 1.0 / np.sqrt(fan_in)
            return jax.random.uniform(key, shape, jnp.float32, -bound, bound)
        key = jax.random.key(seed)
        ks = jax.random.split(key, 7)
        x = jax.random.normal(ks[0], (B, T, D), jnp.float32)
        gate_w = _kaiming_uniform(ks[1], (E, D), D) * 0.01
        w_up = _kaiming_uniform(ks[2], (E, FFN, D), D)
        w_down = _kaiming_uniform(ks[3], (E, D, HALF), HALF)
        sg_gate = _kaiming_uniform(ks[4], (HALF, D), D)
        sg_up = _kaiming_uniform(ks[5], (HALF, D), D)
        sg_down = _kaiming_uniform(ks[6], (D, HALF), HALF)
        return {'x': x, 'gate_w': gate_w, 'w_up': w_up, 'w_down': w_down, 'sg_gate': sg_gate, 'sg_up': sg_up, 'sg_down': sg_down}
    _L0_ffn_in = _L0_ffn_setup()

    def _L1_attn_setup():
        import jax, jax.numpy as jnp
        import numpy as np
        B, S, H, HS, BLK = (4, 1024, 16, 256, 64)
        D = HS // H
        key = jax.random.key(seed)
        ks = jax.random.split(key, 7)
        s = np.float32(1.0 / np.sqrt(HS))
        return {'hidden_states': jax.random.normal(ks[0], (B, S, HS), jnp.float32), 'Wq': jax.random.normal(ks[1], (HS, HS), jnp.float32) * s, 'bq': jax.random.normal(ks[2], (HS,), jnp.float32) * s, 'Wk': jax.random.normal(ks[3], (HS, HS), jnp.float32) * s, 'bk': jax.random.normal(ks[4], (HS,), jnp.float32) * s, 'Wv': jax.random.normal(ks[5], (HS, HS), jnp.float32) * s, 'bv': jax.random.normal(ks[6], (HS,), jnp.float32) * s}
    _L1_attn_in = _L1_attn_setup()

    def _L1_ffn_setup():
        import jax, jax.numpy as jnp
        import numpy as np
        THRESH_FACTOR = 0.7

        def ternary_quantize(w):
            delta = THRESH_FACTOR * jnp.mean(jnp.abs(w))
            return jnp.where(w > delta, 1.0, jnp.where(w < -delta, -1.0, 0.0)).astype(w.dtype)
        key = jax.random.key(seed)
        k1, k2, k3 = jax.random.split(key, 3)
        B, S, D_IN, D_OUT = (8, 1024, 256, 256)
        inp = {'input': jax.random.normal(k1, (B, S, D_IN), dtype=jnp.float32), 'weight': jax.random.normal(k2, (D_OUT, D_IN), dtype=jnp.float32) * (1.0 / np.sqrt(D_IN)), 'alpha': jnp.ones((1,), dtype=jnp.float32), 'bias': jax.random.normal(k3, (D_OUT,), dtype=jnp.float32) * (1.0 / np.sqrt(D_IN))}
        return inp
    _L1_ffn_in = _L1_ffn_setup()
    _d = {'L0_attn_x': _L0_attn_in['x'], 'L0_attn_Wq': _L0_attn_in['Wq'], 'L0_attn_bq': _L0_attn_in['bq'], 'L0_attn_Wk': _L0_attn_in['Wk'], 'L0_attn_bk': _L0_attn_in['bk'], 'L0_attn_Wv': _L0_attn_in['Wv'], 'L0_attn_bv': _L0_attn_in['bv'], 'L0_attn_Wp': _L0_attn_in['Wp'], 'L0_attn_bp': _L0_attn_in['bp'], 'L0_ffn_gate_w': _L0_ffn_in['gate_w'], 'L0_ffn_w_up': _L0_ffn_in['w_up'], 'L0_ffn_w_down': _L0_ffn_in['w_down'], 'L0_ffn_sg_gate': _L0_ffn_in['sg_gate'], 'L0_ffn_sg_up': _L0_ffn_in['sg_up'], 'L0_ffn_sg_down': _L0_ffn_in['sg_down'], 'L1_attn_Wq': _L1_attn_in['Wq'], 'L1_attn_bq': _L1_attn_in['bq'], 'L1_attn_Wk': _L1_attn_in['Wk'], 'L1_attn_bk': _L1_attn_in['bk'], 'L1_attn_Wv': _L1_attn_in['Wv'], 'L1_attn_bv': _L1_attn_in['bv'], 'L1_ffn_weight': _L1_ffn_in['weight'], 'L1_ffn_alpha': _L1_ffn_in['alpha'], 'L1_ffn_bias': _L1_ffn_in['bias']}
    _x0 = _d['L0_attn_x']
    _d['L0_attn_x'] = jax.random.normal(jax.random.fold_in(jax.random.key(seed), 1), (8, 1024, 256), dtype=_x0.dtype)
    del _x0
    return _d

def reference(L0_attn_x, L0_attn_Wq, L0_attn_bq, L0_attn_Wk, L0_attn_bk, L0_attn_Wv, L0_attn_bv, L0_attn_Wp, L0_attn_bp, L0_ffn_gate_w, L0_ffn_w_up, L0_ffn_w_down, L0_ffn_sg_gate, L0_ffn_sg_up, L0_ffn_sg_down, L1_attn_Wq, L1_attn_bq, L1_attn_Wk, L1_attn_bk, L1_attn_Wv, L1_attn_bv, L1_ffn_weight, L1_ffn_alpha, L1_ffn_bias):

    def _L0_attn_ref(x, Wq, bq, Wk, bk, Wv, bv, Wp, bp):
        import jax, jax.numpy as jnp
        import numpy as np
        EMB = 256
        HEADS = 16
        WINDOW = 128
        B, N, E = x.shape
        H = HEADS
        d = E // H

        def proj(W, b):
            y = jnp.einsum('bne,fe->bnf', x, W) + b
            return y.reshape(B, N, H, d).transpose(0, 2, 1, 3)
        q = proj(Wq, bq)
        k = proj(Wk, bk)
        v = proj(Wv, bv)
        energy = jnp.einsum('bhqd,bhkd->bhqk', q, k)
        idx = jnp.arange(N)
        out_of_window = jnp.abs(idx[:, None] - idx[None, :]) > WINDOW
        fmin = jnp.finfo(jnp.float32).min
        energy = jnp.where(out_of_window, fmin, energy)
        scaling = jnp.sqrt(jnp.float32(E))
        att = jax.nn.softmax(energy / scaling, axis=-1)
        out = jnp.einsum('bhqk,bhkd->bhqd', att, v)
        out = out.transpose(0, 2, 1, 3).reshape(B, N, E)
        return jnp.einsum('bne,fe->bnf', out, Wp) + bp

    def _L0_ffn_ref(x, gate_w, w_up, w_down, sg_gate, sg_up, sg_down):
        import jax, jax.numpy as jnp
        import numpy as np
        B, T, D = (4, 1024, 256)
        E = 8
        TOP_K = 2
        FFN = 768
        HALF = FFN // 2

        def _kaiming_uniform(key, shape, fan_in):
            bound = 1.0 / np.sqrt(fan_in)
            return jax.random.uniform(key, shape, jnp.float32, -bound, bound)
        b, t, d = x.shape
        xf = x.reshape(b * t, d)
        N = xf.shape[0]
        logits = xf @ gate_w.T
        topk_logits, topk_idx = jax.lax.top_k(logits, TOP_K)
        topk_w = jax.nn.softmax(topk_logits.astype(jnp.float32), axis=-1).astype(x.dtype)
        comb = jnp.zeros((N, E), x.dtype).at[jnp.arange(N)[:, None], topk_idx].add(topk_w)
        wg = w_up[:, :HALF, :]
        wu = w_up[:, HALF:, :]
        out = jnp.zeros_like(xf)
        for e in range(E):
            g = xf @ wg[e].T
            u = xf @ wu[e].T
            y = jax.nn.silu(g) * u @ w_down[e].T
            out = out + comb[:, e:e + 1] * y
        shared = jax.nn.silu(xf @ sg_gate.T) * (xf @ sg_up.T) @ sg_down.T
        return (shared + out).reshape(b, t, d)

    def _L1_attn_ref(hidden_states, Wq, bq, Wk, bk, Wv, bv):
        import jax, jax.numpy as jnp
        import numpy as np
        B, S, H, HS, BLK = (4, 1024, 16, 256, 64)
        D = HS // H
        b, m, _ = hidden_states.shape
        h, d, wm = (H, D, BLK)
        wn = wm
        nb = m // wm
        scale = np.float32(1.0 / np.sqrt(d))

        def heads(x):
            return x.reshape(b, m, h, d).transpose(0, 2, 1, 3)
        q = heads(hidden_states @ Wq.T + bq)
        k = heads(hidden_states @ Wk.T + bk)
        v = heads(hidden_states @ Wv.T + bv)
        qb = q.reshape(b, h, nb, wm, d)
        kb = k.reshape(b, h, nb, wn, d)
        vb = v.reshape(b, h, nb, wn, d)

        def attend(qx, kx, vx):
            scores = jnp.einsum('bhqd,bhkd->bhqk', qx, kx) * scale
            return jnp.einsum('bhqk,bhkd->bhqd', jax.nn.softmax(scores, axis=-1), vx)
        first_ctx = attend(qb[:, :, 0], k, v)[:, :, None]
        k2 = jnp.concatenate([kb[:, :, 0], kb[:, :, 1], kb[:, :, 2], kb[:, :, -1]], axis=2)
        v2 = jnp.concatenate([vb[:, :, 0], vb[:, :, 1], vb[:, :, 2], vb[:, :, -1]], axis=2)
        second_ctx = attend(qb[:, :, 1], k2, v2)[:, :, None]
        exp_k = jnp.concatenate([kb[:, :, 1:-3], kb[:, :, 2:-2], kb[:, :, 3:-1]], axis=3)
        exp_v = jnp.concatenate([vb[:, :, 1:-3], vb[:, :, 2:-2], vb[:, :, 3:-1]], axis=3)
        mq = qb[:, :, 2:-2]
        inner = jnp.einsum('bhlqd,bhlkd->bhlqk', mq, exp_k) * scale
        first_band = jnp.einsum('bhlqd,bhkd->bhlqk', mq, kb[:, :, 0]) * scale
        last_band = jnp.einsum('bhlqd,bhkd->bhlqk', mq, kb[:, :, -1]) * scale
        band = jnp.concatenate([first_band, inner, last_band], axis=-1)
        aw = jax.nn.softmax(band, axis=-1)
        mid_ctx = jnp.einsum('bhlqk,bhlkd->bhlqd', aw[..., wn:4 * wn], exp_v)
        mid_ctx = mid_ctx + jnp.einsum('bhlqk,bhkd->bhlqd', aw[..., :wn], vb[:, :, 0])
        mid_ctx = mid_ctx + jnp.einsum('bhlqk,bhkd->bhlqd', aw[..., -wn:], vb[:, :, -1])
        k3 = jnp.concatenate([kb[:, :, 0], kb[:, :, -3], kb[:, :, -2], kb[:, :, -1]], axis=2)
        v3 = jnp.concatenate([vb[:, :, 0], vb[:, :, -3], vb[:, :, -2], vb[:, :, -1]], axis=2)
        second_last_ctx = attend(qb[:, :, -2], k3, v3)[:, :, None]
        last_ctx = attend(qb[:, :, -1], k, v)[:, :, None]
        ctx = jnp.concatenate([first_ctx, second_ctx, mid_ctx, second_last_ctx, last_ctx], axis=2)
        return ctx.reshape(b, h, m, d).transpose(0, 2, 1, 3).reshape(b, m, h * d)

    def _L1_ffn_ref(input, weight, alpha, bias):
        import jax, jax.numpy as jnp
        import numpy as np
        THRESH_FACTOR = 0.7

        def ternary_quantize(w):
            delta = THRESH_FACTOR * jnp.mean(jnp.abs(w))
            return jnp.where(w > delta, 1.0, jnp.where(w < -delta, -1.0, 0.0)).astype(w.dtype)
        w_ternary = ternary_quantize(weight)
        w_eff = w_ternary * alpha
        out = jnp.einsum('bsd,od->bso', input, w_eff) + bias
        return out
    x = L0_attn_x
    x = x + _L0_attn_ref(_layernorm(x, axis=-1), L0_attn_Wq, L0_attn_bq, L0_attn_Wk, L0_attn_bk, L0_attn_Wv, L0_attn_bv, L0_attn_Wp, L0_attn_bp)
    x = x + _L0_ffn_ref(_layernorm(x, axis=-1), L0_ffn_gate_w, L0_ffn_w_up, L0_ffn_w_down, L0_ffn_sg_gate, L0_ffn_sg_up, L0_ffn_sg_down)
    x = x + _L1_attn_ref(_layernorm(x, axis=-1), L1_attn_Wq, L1_attn_bq, L1_attn_Wk, L1_attn_bk, L1_attn_Wv, L1_attn_bv)
    x = x + _L1_ffn_ref(_layernorm(x, axis=-1), L1_ffn_weight, L1_ffn_alpha, L1_ffn_bias)
    return x

_drawn_inputs = setup_inputs


def setup_inputs(seed=0):
    import zlib

    import numpy as np

    out = dict(_drawn_inputs(seed))
    spreads = {'L0_attn_bq': (0.0, 0.8),
     'L0_attn_bk': (0.0, 0.8),
     'L0_attn_bv': (0.0, 0.1),
     'L0_attn_bp': (0.0, 0.1)}
    factors = {'L0_attn_Wq': 8.0,
     'L0_attn_Wk': 8.0,
     'L0_attn_Wv': 5.86,
     'L1_attn_bq': 8.0,
     'L1_attn_bk': 8.0,
     'L1_ffn_bias': 8.0}
    for name, (base, spread) in spreads.items():
        noise = np.random.default_rng([zlib.crc32(name.encode()), seed]).standard_normal(out[name].shape)
        drawn = base * np.exp(spread * noise) if base else spread * noise
        out[name] = jnp.asarray(drawn.astype(out[name].dtype))
    for name, factor in factors.items():
        out[name] = (out[name] * factor).astype(out[name].dtype)
    return out
```

```python
from contextlib import ExitStack

import numpy as np

import concourse.bass as bass
from concourse import mybir

ALU = mybir.AluOpType
ACT = mybir.ActivationFunctionType
AXX = mybir.AxisListType.X
F32 = mybir.dt.float32
F16 = mybir.dt.float16
BF16 = mybir.dt.bfloat16
U32 = mybir.dt.uint32

P = 128
B, N, D = 8, 1024, 256
T = B * N
NT = T // P
TB = N // P
CH = 512
NC = T // CH
TC = CH // P
EC = D // P
H, DH = 16, 16
HG = 4
VW = DH + 1
TR = 3 * DH + 1
E = 8
F = 384
FC = F // P
EPS = 1e-5
ONE = 1

XS = 256.0
WS = 256.0
PS = 1.0 / (XS * WS)
QS = 16.0
MROW = 32768.0
AS = 64.0
HS = 64.0
YS = 1.0 / (HS * WS)
NEG = -1e30


def chunk_pipeline(eng, front, main):
    front(0, 0, 0)
    with eng.Fori(0, NC // 2 - 1) as i:
        front(i * 2 + 1, 1, i)
        main(i * 2, 0, i)
        front(i * 2 + 2, 0, i + 1)
        main(i * 2 + 1, 1, i)
    last = NC // 2 - 1
    front(NC - 1, 1, last)
    main(NC - 2, 0, last)
    main(NC - 1, 1, last)


def heads(ap, width):
    return ap.rearrange("p t (h w) -> p (t h) w", w=width)


def split3(pe, out, stat_hi, stat_lo, mov_hi, mov_lo, parts, skip=False):
    n = len(parts)
    for a, p in enumerate(parts):
        pe.matmul(out, stat_hi(p), mov_hi(p), start=(a == 0), stop=False)
        pe.matmul(out, stat_hi(p), mov_lo(p), start=False, stop=False)
        last = pe.matmul(out, stat_lo(p), mov_hi(p), start=False, stop=(a == n - 1))
    return last


class Semaphores:

    def __init__(self, nc, ctx, tag):
        self.nc, self.ctx, self.tag, self.taken = nc, ctx, tag, []
        ctx.callback(self.clear)

    def __call__(self, name):
        self.taken.append(self.ctx.enter_context(self.nc.semaphore(f"{self.tag}_{name}")))
        return self.taken[-1]

    def start(self):
        with self.nc.Block() as block:
            @block.gpsimd
            def _(pool):
                for s in self.taken:
                    pool.sem_inc(s, ONE)

    def clear(self):
        with self.nc.Block() as block:
            @block.gpsimd
            def _(pool):
                for s in self.taken:
                    pool.sem_clear(s)


def after(eng, sem, value):
    if not isinstance(value, int) or value > 0:
        eng.wait_ge(sem, ONE + value)


def stage_stats(nc, tag, x_dram, x_res, mean, rstd, permuted):
    with ExitStack() as ctx:
        sem = Semaphores(nc, ctx, tag)
        ld = [sem(f"ld{b}") for b in range(B)]
        stats = Stats(nc, ctx, sem, tag, mean, rstd)
        sem.start()
        block = ctx.enter_context(nc.Block())
        n_dma = 3 if permuted else 1

        @block.sync
        def _(sp):
            for b in range(B):
                xb = x_dram[b * N:(b + 1) * N, :]
                if permuted:
                    sp.dma_start(x_res[0:64, b * TB, :], xb[0:64, :]).then_inc(ld[b], 16)
                    sp.dma_start(x_res[64:128, b * TB, :], xb[N - 64:N, :]).then_inc(ld[b], 16)
                    sp.dma_start(x_res[:, b * TB + 1:(b + 1) * TB, :],
                                 xb[64:N - 64, :].rearrange("(t p) d -> p t d", p=P)).then_inc(ld[b], 16)
                else:
                    sp.dma_start(x_res[:, b * TB:(b + 1) * TB, :],
                                 xb.rearrange("(t p) d -> p t d", p=P)).then_inc(ld[b], 16)

        @block.vector
        def _(dve):
            for b in range(B):
                dve.wait_ge(ld[b], ONE + 16 * n_dma)
                with dve.Fori(0, TB) as t:
                    stats.tile(dve, x_res, t + b * TB)
            stats.finish(dve)

        @block.scalar
        def _(act):
            stats.root(act)


class Stats:

    def __init__(self, nc, ctx, sem, tag, mean, rstd):
        self.st = ctx.enter_context(nc.sbuf_tensor(f"{tag}_st", [P, NT, 6], F32))
        self.tmp = ctx.enter_context(nc.sbuf_tensor(f"{tag}_tmp", [P, 6, NT], F32))
        self.mean, self.rstd = mean, rstd
        self.bn, self.step, self.std_done = sem("bn"), sem("stat_step"), sem("std_done")

    def tile(self, dve, x_res, ti):
        dve.bn_stats(self.st[:, ti, :], x_res[:, ti, :]).then_inc(self.bn, 1)

    def finish(self, dve):
        st = self.st
        total, apart, var, apart2, var2, std = (self.tmp[:, n, :] for n in range(6))
        dve.wait_ge(self.bn, ONE + NT)
        dve.tensor_tensor(total, st[:, :, 1], st[:, :, 4], ALU.add).then_inc(self.step, 1)
        dve.tensor_tensor(apart, st[:, :, 1], st[:, :, 4], ALU.subtract).then_inc(self.step, 1)
        dve.tensor_tensor(var, st[:, :, 2], st[:, :, 5], ALU.add).then_inc(self.step, 1)
        dve.wait_ge(self.step, ONE + 3)
        dve.tensor_scalar(self.mean[:, :], total, 0.5, None, ALU.mult).then_inc(self.step, 1)
        dve.scalar_tensor_tensor(out=apart2, in0=apart, scalar=0.25, in1=apart, op0=ALU.mult, op1=ALU.mult)\
           .then_inc(self.step, 1)
        dve.tensor_scalar(var, var, 1.0 / D, EPS, ALU.mult, ALU.add).then_inc(self.step, 1)
        dve.wait_ge(self.step, ONE + 6)
        dve.tensor_tensor(var2, var, apart2, ALU.add).then_inc(self.step, 1)
        dve.wait_ge(self.std_done, ONE + 1)
        dve.reciprocal(self.rstd[:, :], std).then_inc(self.step, 1)

    def root(self, act):
        act.wait_ge(self.step, ONE + 7)
        act.activation(self.tmp[:, 5, :], self.tmp[:, 4, :], ACT.Sqrt).then_inc(self.std_done, 1)


class Front:

    def __init__(self, nc, ctx, sem, tag, x_res, mean, rstd, ident, xh, xl):
        self.x_res, self.mean, self.rstd, self.ident = x_res, mean, rstd, ident
        self.xn = ctx.enter_context(nc.sbuf_tensor(f"{tag}_xn", [P, 2, TC, D], F32))
        self.pt = [ctx.enter_context(nc.psum_tensor(f"{tag}_pt{e}", [P, CH], F32)) for e in range(EC)]
        self.xh, self.xl = xh, xl
        self.normed = [sem(f"normed{k}") for k in range(2)]
        self.transposed = [sem(f"transposed{e}") for e in range(EC)]
        self.hi_done = [sem(f"hi_done{e}") for e in range(EC)]
        self.lo_done = [sem(f"lo_done{e}") for e in range(EC)]

    def norm_next(self, dve, c, k, i):
        if not isinstance(c, int) or c < NC - 1:
            self.norm(dve, c + 1, 1 - k, i + k)

    def norm(self, dve, c, k, i):
        after(dve, self.transposed[EC - 1], c - 1)
        for t in range(TC):
            ti = c * TC + t
            dve.tensor_scalar(self.xn[:, k, t, :], self.x_res[:, ti, :], self.mean[:, bass.ds(ti, 1)],
                              self.rstd[:, bass.ds(ti, 1)], ALU.subtract, ALU.mult).then_inc(self.normed[k], 1)

    def transpose(self, pe, c, k, i):
        pe.wait_ge(self.normed[k], ONE + i * TC + TC)
        for e in range(EC):
            pe.wait_ge(self.lo_done[e], ONE + c)
            for t in range(TC):
                last = pe.transpose(self.pt[e][:, t * P:(t + 1) * P],
                                    self.xn[:, k, t, e * P:(e + 1) * P], self.ident[:, :])
            last.then_inc(self.transposed[e], 1)

    def hi(self, act, c, k, i, extra=None):
        if extra:
            extra(act, c, k, i)
        for e in range(EC):
            act.wait_ge(self.transposed[e], ONE + c + 1)
            act.activation(self.xh(c, k)[:, e, :], self.pt[e][:, :], ACT.Copy, scale=XS)\
               .then_inc(self.hi_done[e], 1)

    def lo(self, dve, c, k, i):
        for e in range(EC):
            dve.wait_ge(self.hi_done[e], ONE + c + 1)
            dve.scalar_tensor_tensor(out=self.xl(c, k)[:, e, :], in0=self.pt[e][:, :], scalar=XS,
                                     in1=self.xh(c, k)[:, e, :], op0=ALU.mult, op1=ALU.subtract)\
               .then_inc(self.lo_done[e], 1)

    def split_ready(self, eng, c):
        for e in range(EC):
            eng.wait_ge(self.lo_done[e], ONE + c + 1)


def stage_project(nc, tag, x_res, mean, rstd, ident, w_in, b_in, qx, kx, vx):
    with ExitStack() as ctx:
        def sb(n, shape, dt):
            return ctx.enter_context(nc.sbuf_tensor(f"{tag}_{n}", shape, dt))

        sem = Semaphores(nc, ctx, tag)

        w32 = sb("w32", [P, 3, EC, D], F32)
        wh = sb("wh", [P, 3, EC, D], F16)
        wl = sb("wl", [P, 3, EC, D], F16)
        bqk = sb("bqk", [P, 4], F32)
        bqk_s = sb("bqk_s", [P, 4], F32)
        bv = sb("bv", [P, 2, D], F32)
        xh = sb("xh", [P, 2, EC, CH], F16)
        xl = sb("xl", [P, 2, EC, CH], F16)
        qk32 = sb("qk32", [P, 2, CH], F32)
        stg = sb("stg", [P, 2, 4, 2, CH], F16)
        vst = sb("vst", [P, 2, TC, H * VW], F32)
        pqk = [ctx.enter_context(nc.psum_tensor(f"{tag}_pqk{m}", [P, CH], F32)) for m in range(4)]
        pv = [ctx.enter_context(nc.psum_tensor(f"{tag}_pv{m}", [P, 2, D], F32)) for m in range(2)]
        fr = Front(nc, ctx, sem, tag, x_res, mean, rstd, ident, lambda c, k: xh[:, k], lambda c, k: xl[:, k])
        s_w, s_wh, s_wl, s_bqk, s_ones = sem("w"), sem("whi"), sem("wlo"), sem("bqk_ready"), sem("ones")
        qk_ready = [sem(f"qk_ready{m}") for m in range(4)]
        qk_copied = [sem(f"qk_copied{m}") for m in range(4)]
        qk_hi = [sem(f"qk_hi{m}") for m in range(2)]
        qk_lo = [sem(f"qk_lo{m}") for m in range(2)]
        v_ready = [sem(f"v_ready{m}") for m in range(2)]
        v_copied = [sem(f"v_copied{m}") for m in range(2)]
        stored = [sem(f"stored{k}") for k in range(2)]
        n_store = 2 * 2 * 3 + 1
        sem.start()
        block = ctx.enter_context(nc.Block())

        @block.sync
        def _(sp):
            sp.dma_start(w32[:, :, :, :], w_in).then_inc(s_w, 16)
            sp.dma_start(bqk[:, :], b_in[0]).then_inc(s_w, 16)
            for r in range(2):
                sp.dma_start(bv[:, r, :], b_in[1].partition_broadcast(P)).then_inc(s_w, 16)

            def front(c, k, i):
                pass

            def main(c, k, i):
                for m in range(2):
                    sp.wait_ge(qk_lo[m], ONE + c * 2 + 2)
                tok = c * CH
                for m in range(4):
                    x, g0 = (qx, kx)[m // 2], 4 * (m % 2)
                    for term, part in enumerate(((0, 0, 1), (0, 1, 0))[m // 2]):
                        sp.dma_start(x[g0:g0 + 4, term * DH:(term + 1) * DH, :, bass.ds(tok, CH)]
                                     .rearrange("g d i t -> g (d i) t"),
                                     stg[:, k, m, part, :]).then_inc(stored[k], 16)
                for m in range(2):
                    sp.wait_ge(v_copied[m], ONE + c + 1)
                sp.dma_start(vx[bass.ds(tok, CH), :].rearrange("(t p) w -> p t w", p=P),
                             vst[:, k, :, :]).then_inc(stored[k], 16)

            chunk_pipeline(sp, front, main)
            for k in range(2):
                sp.wait_ge(stored[k], ONE + NC // 2 * n_store * 16)

        @block.vector
        def _(dve):
            dve.memset(vst[:, :, :, :], 1.0).then_inc(s_ones, 1)
            dve.wait_ge(s_w, ONE + 64)
            dve.tensor_scalar(bqk_s[:, :], bqk[:, :], QS, None, ALU.mult).then_inc(s_bqk, 1)
            for j in range(3):
                dve.wait_ge(s_wh, ONE + j + 1)
                dve.scalar_tensor_tensor(out=wl[:, j], in0=w32[:, j], scalar=WS, in1=wh[:, j],
                                         op0=ALU.mult, op1=ALU.subtract).then_inc(s_wl, 1)
            dve.wait_ge(s_ones, ONE + 1)

            def front(c, k, i):
                after(dve, v_ready[1], c - 1)
                fr.lo(dve, c, k, i)
                fr.norm_next(dve, c, k, i)

            def main(c, k, i):
                dve.wait_ge(stored[k], ONE + i * (n_store * 16))
                for m in range(4):
                    dve.wait_ge(qk_copied[m], ONE + c + 1)
                    dve.tensor_copy(stg[:, k, m, 0, :], qk32[:, m % 2, :]).then_inc(qk_hi[m % 2], 1)
                for m in range(2):
                    dve.wait_ge(v_ready[m], ONE + c + 1)
                    dve.scalar_tensor_tensor(out=heads(vst[:, k, 2 * m:2 * m + 2, :], VW)[:, :, 0:DH],
                                             in0=heads(pv[m][:, :, :], DH), scalar=PS, in1=heads(bv[:, :, :], DH),
                                             op0=ALU.mult, op1=ALU.add).then_inc(v_copied[m], 1)

            fr.norm(dve, 0, 0, 0)
            chunk_pipeline(dve, front, main)

        @block.gpsimd
        def _(pool):
            def front(c, k, i):
                pass

            def main(c, k, i):
                for m in range(4):
                    pool.wait_ge(qk_hi[m % 2], ONE + c * 2 + (m // 2 + 1))
                    pool.tensor_tensor(stg[:, k, m, 1, :], qk32[:, m % 2, :], stg[:, k, m, 0, :],
                                       ALU.subtract).then_inc(qk_lo[m % 2], 1)

            chunk_pipeline(pool, front, main)

        @block.scalar
        def _(act):
            act.wait_ge(s_w, ONE + 64)
            for j in range(3):
                act.activation(wh[:, j], w32[:, j], ACT.Copy, scale=WS).then_inc(s_wh, 1)
            act.wait_ge(s_bqk, ONE + 1)

            def front(c, k, i):
                after(act, v_ready[1], c - 1)
                fr.hi(act, c, k, i)

            def main(c, k, i):
                for m in range(4):
                    act.wait_ge(qk_ready[m], ONE + c + 1)
                    act.wait_ge(qk_lo[m % 2], ONE + c * 2 + m // 2)
                    act.activation(qk32[:, m % 2, :], pqk[m][:, :], ACT.Identity, bias=bqk_s[:, m:m + 1],
                                   scale=QS * PS).then_inc(qk_copied[m], 1)

            chunk_pipeline(act, front, main)

        @block.tensor
        def _(pe):
            pe.wait_ge(s_wl, ONE + 3)

            def front(c, k, i):
                fr.transpose(pe, c, k, i)

            def main(c, k, i):
                fr.split_ready(pe, c)
                for m in range(4):
                    pe.wait_ge(qk_copied[m], ONE + c)
                    j, cols = m // 2, slice((m % 2) * P, (m % 2) * P + P)
                    split3(pe, pqk[m][:, :], lambda e: wh[:, j, e, cols], lambda e: wl[:, j, e, cols],
                           lambda e: xh[:, k, e, :], lambda e: xl[:, k, e, :], range(EC))\
                        .then_inc(qk_ready[m], 1)
                for m in range(2):
                    pe.wait_ge(v_copied[m], ONE + c)
                    for s in range(2):
                        t = 2 * m + s
                        last = split3(pe, pv[m][:, s, :], lambda e: xh[:, k, e, t * P:(t + 1) * P],
                                      lambda e: xl[:, k, e, t * P:(t + 1) * P],
                                      lambda e: wh[:, 2, e, :], lambda e: wl[:, 2, e, :], range(EC))
                    last.then_inc(v_ready[m], 1)

            chunk_pipeline(pe, front, main)




def window_jobs():
    jobs = []
    for t in range(TB):
        lo, hi = max(0, t - 1), min(TB, t + 2)
        masks = []
        if t > 0:
            masks.append((0, P, 0))
        if t < TB - 1:
            masks.append(((hi - lo - 1) * P, P, 1))
        jobs.append((t, [(lo * P, (hi - lo) * P, 0)], masks))
    return jobs


def block_jobs():
    jobs = [(0, [(0, 512, 0)], []), (0, [(512, 512, 0)], [])]
    for t in range(1, TB):
        lo, hi = max(P, t * P - 64), min(N, t * P + P + 64)
        jobs.append((t, [(0, P, 0), (lo, hi - lo, P)], []))
    return jobs


def block_rows():
    rows = np.zeros((2, 4, N), np.float16)
    for n in range(2, N // 64):
        rows[0, (n + 2) % 4, n * 64:(n + 1) * 64] = -65504.0
        rows[1, n % 4, n * 64:(n + 1) * 64] = MROW
    return rows


def stage_attend(nc, tag, jobs, scale, identb, masks, const_rows, ident16, qx, kx, vx, ox):
    nj = len(jobs)
    n_s = 4 * nj
    with ExitStack() as ctx:
        def sb(n, shape, dt):
            return ctx.enter_context(nc.sbuf_tensor(f"{tag}_{n}", shape, dt))

        sem = Semaphores(nc, ctx, tag)

        qe = [sb(f"qe{g}", [P, 2, 2, N], F16) for g in range(HG)]
        ke = [sb(f"ke{g}", [P, 2, N], F16) for g in range(HG)]
        ve = [sb(f"ve{g}", [P, TB, 4 * VW], F32) for g in range(HG)]
        pr = [sb(f"pr{s}", [P, 2, 2, CH], F32) for s in range(2)]
        mx = sb("mx", [P, 2, 2, TB], F32)
        mx2 = sb("mx2", [P, 2, 2, 2], F32)
        mneg = sb("mneg", [P, 2 * 2 * TB], F16)
        mt = [sb(f"mt{s}", [2 * 2 * TB, P], F16) for s in range(2)]
        ost = [sb(f"ost{s}", [P, N], F32) for s in range(2)]
        psc = [ctx.enter_context(nc.psum_tensor(f"{tag}_psc{s}", [P, CH], F32)) for s in range(2)]
        pst = ctx.enter_context(nc.psum_tensor(f"{tag}_pst", [P, 2, 2, CH], F32))
        po = ctx.enter_context(nc.psum_tensor(f"{tag}_po", [P, N], F32))
        zeroed, rows_set = sem("zeroed"), sem("rows_set")
        loaded = [sem(f"loaded{g}") for g in range(HG)]
        s_ready = [sem(f"s_ready{s}") for s in range(2)]
        s_read = [sem(f"s_read{s}") for s in range(2)]
        m_done = sem("m_done")
        m_neg = sem("m_neg")
        m_turned = sem("m_turned")
        m_copied = sem("m_copied")
        m_loaded = [sem(f"m_loaded{g}") for g in range(HG)]
        t_ready = [sem(f"t_ready{i}") for i in range(2)]
        p_ready = [sem(f"p_ready{i}") for i in range(2)]
        p_used = [sem(f"p_used{s}") for s in range(2)]
        o_copied = sem("o_copied")
        o_stored = [sem(f"o_stored{s}") for s in range(2)]
        two_part = len([1 for t, _, _ in jobs if t == 0]) == 2
        N_LOAD = 5
        sem.start()
        block = ctx.enter_context(nc.Block())

        def unit_pipeline(eng, scores, attend, both):
            scores(0, 0)
            scores(1, 0)
            with eng.Fori(0, B - 1) as b:
                for g in range(HG):
                    both((g + 2, b) if g < 2 else (g - 2, b + 1), (g, b))
            for g in range(HG):
                both((g + 2, B - 1) if g < 2 else None, (g, B - 1))

        def p_slot(g, b, s):
            n = g * nj + s
            return n % 2, b * (HG * nj // 2) + n // 2

        def wait_unit(eng, g, b):
            slot, use = p_slot(g, b, nj - 1)
            eng.wait_ge(p_used[slot], ONE + use + 1)

        @block.sync
        def _(sp):
            def load(g, b):
                tok = b * N
                for par in range(2):
                    sp.dma_start(qe[g][par * 64:par * 64 + TR, par, :, :], qx[2 * g + par, :, :, bass.ds(tok, N)])\
                        .then_inc(loaded[g], 16)
                    sp.dma_start(ke[g][par * 64:par * 64 + TR, :, :], kx[2 * g + par, :, :, bass.ds(tok, N)])\
                        .then_inc(loaded[g], 16)
                sp.dma_start(ve[g][:, :, :], vx[bass.ds(tok, N), g * 4 * VW:(g + 1) * 4 * VW]
                             .rearrange("(t p) w -> p t w", p=P)).then_inc(loaded[g], 16)

            def scores(g, b):
                sp.wait_ge(m_copied, ONE + b * HG + g + 1)
                for par in range(2):
                    for i in range(2):
                        r = (par * 2 + i) * TB
                        sp.dma_start(qe[g][par * 64 + TR - 1:par * 64 + TR, par, i, :]
                                     .rearrange("o (t c) -> o t c", c=P),
                                     mt[g % 2][r:r + TB, :]).then_inc(m_loaded[g], 16)

            def both(nxt, cur):
                if nxt:
                    scores(*nxt)
                g, b = cur
                wait_unit(sp, g, b)
                if not isinstance(b, int):
                    load(g, b + 1)
                sp.wait_ge(o_copied, ONE + (b * HG + g) * 2 + 2)
                for h in range(4):
                    sp.dma_start(ox[g, h * VW:(h + 1) * VW, bass.ds(b * N, N)],
                                 ost[g % 2][32 * h:32 * h + VW, :]).then_inc(o_stored[g % 2], 16)

            sp.wait_ge(zeroed, ONE + 2 * HG)
            if const_rows is not None:
                for g in range(HG):
                    for par in range(2):
                        for i in range(2):
                            r = slice(par * 64 + TR, par * 64 + TR + 4)
                            sp.dma_start(qe[g][r, par, i, :], const_rows[0]).then_inc(rows_set, 16)
                            sp.dma_start(ke[g][r, i, :], const_rows[1]).then_inc(rows_set, 16)
            for g in range(HG):
                load(g, 0)
            unit_pipeline(sp, scores, None, both)
            for s in range(2):
                sp.wait_ge(o_stored[s], ONE + B * HG // 2 * 64)

        @block.gpsimd
        def _(pool):
            for g in range(HG):
                pool.memset(qe[g][:, :, :, :].rearrange("p a i t -> p (a i t)").bitcast(U32), 0).then_inc(zeroed, 1)
                pool.memset(ke[g][:, :, :].rearrange("p i t -> p (i t)").bitcast(U32), 0).then_inc(zeroed, 1)

        @block.vector
        def _(dve):
            dve.memset(po[:, :], 0.0).then_inc(m_done, 1)

            def scores(g, b):
                u = b * HG + g
                for n in range(n_s):
                    j, h = divmod(n, 4)
                    par, i = h % 2, h // 2
                    t, pieces, _m = jobs[j]
                    width = sum(p[1] for p in pieces)
                    dve.wait_ge(s_ready[n % 2], ONE + u * (n_s // 2) + n // 2 + 1)
                    out = mx2[:, par, i, j:j + 1] if two_part and t == 0 else mx[:, par, i, t:t + 1]
                    dve.tensor_reduce(out, psc[n % 2][:, 0:width], AXX, ALU.max).then_inc(s_read[n % 2], 1)
                for s in range(2):
                    dve.wait_ge(s_read[s], ONE + (u + 1) * (n_s // 2))
                if two_part:
                    dve.tensor_tensor(mx[:, :, :, 0], mx2[:, :, :, 0], mx2[:, :, :, 1], ALU.max)\
                       .then_inc(m_done, 1)
                    dve.wait_ge(m_done, ONE + u + 2)
                dve.wait_ge(m_turned, ONE + u)
                dve.tensor_scalar(mneg[:, :], mx[:, :, :, :].rearrange("p a i t -> p (a i t)"),
                                  -1.0 / MROW, None, ALU.mult).then_inc(m_neg, 1)

            def both(nxt, cur):
                if nxt:
                    scores(*nxt)

            unit_pipeline(dve, scores, None, both)

        @block.scalar
        def _(act):
            def turn(g, b):
                u = b * HG + g
                act.wait_ge(m_turned, ONE + u + 1)
                after(act, m_loaded[(g + 2) % HG], b * 64 + (g // 2) * 64)
                act.activation(mt[g % 2][:, :], psc[0][0:4 * TB, 0:P // 2].bitcast(F16), ACT.Copy)\
                   .then_inc(m_copied, 1)

            def both(nxt, cur):
                g, b = cur
                u = b * HG + g
                for s in range(nj):
                    t, pieces, _m = jobs[s]
                    width = sum(p[1] for p in pieces)
                    slot, use = p_slot(g, b, s)
                    act.wait_ge(p_used[slot], ONE + use)
                    for i in range(2):
                        act.wait_ge(t_ready[i], ONE + u * nj + s + 1)
                        act.activation(pr[slot][:, i, :, 0:width], pst[:, i, :, 0:width], ACT.Exp, scale=scale)\
                           .then_inc(p_ready[i], 1)
                if nxt:
                    turn(*nxt)
                act.wait_ge(o_stored[g % 2], ONE + b * 128 + (g // 2) * 64)
                wait_unit(act, g, b)
                for half in range(2):
                    act.activation(ost[g % 2][:, half * CH:(half + 1) * CH], po[:, half * CH:(half + 1) * CH],
                                   ACT.Copy).then_inc(o_copied, 1)

            unit_pipeline(act, turn, None, both)

        @block.tensor
        def _(pe):
            pe.wait_ge(m_done, ONE + 1)
            if const_rows is not None:
                pe.wait_ge(rows_set, ONE + HG * 8 * 16)

            def product(out, stat, mov, pieces, mask_list):
                for n, (tok, count, col) in enumerate(pieces):
                    last = pe.matmul(out[:, col:col + count], stat, mov(tok, count), start=(n == 0),
                                     stop=(n == len(pieces) - 1 and not mask_list), skip_group_check=True)
                for n, (col, width, which) in enumerate(mask_list):
                    last = pe.matmul(out[:, col:col + width], identb[:, :], masks[:, which, 0:width],
                                     start=False, stop=(n == len(mask_list) - 1), skip_group_check=True)
                return last

            def score(g, b, n):
                u = b * HG + g
                j, h = divmod(n, 4)
                par, i = h % 2, h // 2
                t, pieces, mask_list = jobs[j]
                if n == 0:
                    pe.wait_ge(loaded[g], ONE + b * (N_LOAD * 16) + N_LOAD * 16)
                    pe.wait_ge(m_copied, ONE + u)
                pe.wait_ge(s_read[n % 2], ONE + u * (n_s // 2) + n // 2)
                product(psc[n % 2], qe[g][:, par, i, t * P:(t + 1) * P],
                        lambda tok, count: ke[g][:, i, tok:tok + count], pieces, mask_list)\
                    .then_inc(s_ready[n % 2], 1)

            def turn(g, b):
                u = b * HG + g
                pe.wait_ge(m_neg, ONE + u + 1)
                pe.transpose(psc[0][0:4 * TB, 0:P // 2].bitcast(F16), mneg[:, :], ident16[:, :])\
                  .then_inc(m_turned, 1)

            def scores(g, b):
                for n in range(n_s):
                    score(g, b, n)
                turn(g, b)

            written = {}

            def with_v(g, b, s):
                t, pieces, _m = jobs[s]
                slot, use = p_slot(g, b, s)
                u = b * HG + g
                if s == 0:
                    written.clear()
                    pe.wait_ge(o_copied, ONE + u * 2)
                for i in range(2):
                    pe.wait_ge(p_ready[i], ONE + u * nj + s + 1)
                cuts = []
                for tok, count, col in pieces:
                    while count:
                        w = min(count, CH - tok % CH)
                        cuts.append((tok, w, col))
                        tok, count, col = tok + w, count - w, col + w
                for tok, w, col in cuts:
                    for h in range(4):
                        par, i = h % 2, h // 2
                        first = (h, tok // CH) not in written
                        written[(h, tok // CH)] = True
                        last = pe.matmul(po[32 * h:32 * h + VW, tok:tok + w], ve[g][:, t, h * VW:(h + 1) * VW],
                                         pr[slot][:, i, par, col:col + w], start=first, stop=(s == nj - 1),
                                         skip_group_check=True, tile_position=(0, 32 * h))
                return last

            def both(nxt, cur):
                g, b = cur
                u = b * HG + g
                ahead = list(range(n_s)) if nxt else []

                def one_score():
                    if ahead:
                        score(*nxt, ahead.pop(0))

                for s in range(nj + 1):
                    if s < nj:
                        t, pieces, mask_list = jobs[s]
                        if s == 0:
                            pe.wait_ge(m_loaded[g], ONE + b * 64 + 64)
                        for i in range(2):
                            pe.wait_ge(p_ready[i], ONE + u * nj + s)
                            for par in range(2):
                                last = product(pst[:, i, par, :], ke[g][:, i, t * P:(t + 1) * P],
                                               lambda tok, count: qe[g][:, par, i, tok:tok + count],
                                               pieces, mask_list)
                                if par == 1:
                                    last.then_inc(t_ready[i], 1)
                                if (i, par) != (0, 0):
                                    one_score()
                    if s > 0:
                        with_v(g, b, s - 1).then_inc(p_used[p_slot(g, b, s - 1)[0]], 1)
                    if s < nj:
                        one_score()
                if nxt:
                    turn(*nxt)

            unit_pipeline(pe, scores, None, both)


def stage_combine(nc, tag, x_res, mean, rstd, ident, ox, wp_in, bp_in):
    with ExitStack() as ctx:
        def sb(n, shape, dt):
            return ctx.enter_context(nc.sbuf_tensor(f"{tag}_{n}", shape, dt))

        sem = Semaphores(nc, ctx, tag)

        project = wp_in is not None
        ot = sb("ot", [4 * VW, 2, HG, CH], F32)
        rec = sb("rec", [P, 2, H], F32)
        att = sb("att", [P, 2, TC, D], F32)
        stats = Stats(nc, ctx, sem, tag, mean, rstd)
        pt = [ctx.enter_context(nc.psum_tensor(f"{tag}_ptok{s}", [P, CH], F32)) for s in range(2)]
        loaded = [sem(f"loaded{k}") for k in range(2)]
        turned = [sem(f"turned{s}") for s in range(2)]
        rec_done = sem("rec_done")
        pt_read = [sem(f"pt_read{s}") for s in range(2)]
        x_done = sem("x_done")
        if project:
            w32 = sb("w32", [P, EC, D], F32)
            wh, wl = sb("wh", [P, EC, D], F16), sb("wl", [P, EC, D], F16)
            bp = sb("bp", [P, D], F32)
            ah, al = sb("ah", [P, EC, CH], F16), sb("al", [P, EC, CH], F16)
            pe_t = [ctx.enter_context(nc.psum_tensor(f"{tag}_pet{e}", [P, CH], F32)) for e in range(EC)]
            py = [ctx.enter_context(nc.psum_tensor(f"{tag}_py{s}", [P, 2, D], F32)) for s in range(2)]
            s_w, s_wh, s_wl, biased = sem("w"), sem("whi"), sem("wlo"), sem("biased")
            att_turned = [sem(f"att_turned{e}") for e in range(EC)]
            a_hi, a_lo = [sem(f"a_hi{e}") for e in range(EC)], [sem(f"a_lo{e}") for e in range(EC)]
            y_ready = [sem(f"y_ready{s}") for s in range(2)]
            y_read = [sem(f"y_read{s}") for s in range(2)]
        sem.start()
        block = ctx.enter_context(nc.Block())

        @block.sync
        def _(sp):
            if project:
                sp.dma_start(w32[:, :, :], wp_in).then_inc(s_w, 16)
                sp.dma_start(bp[:, :], bp_in.partition_broadcast(P)).then_inc(s_w, 16)

            def front(c, k, i):
                after(sp, turned[1], (c - 1) * 2)
                sp.dma_start(ot[:, k, :, :], ox[:, :, bass.ds(c * CH, CH)].rearrange("g r t -> r g t"))\
                  .then_inc(loaded[k], 16)

            chunk_pipeline(sp, front, lambda c, k, i: None)

        @block.tensor
        def _(pe):
            if project:
                pe.wait_ge(s_wl, ONE + 1)

            def front(c, k, i):
                pe.wait_ge(loaded[k], ONE + i * 16 + 16)
                for t in range(TC):
                    pe.wait_ge(pt_read[t % 2], ONE + c * 2 + t // 2)
                    for g in range(HG):
                        last = pe.transpose(pt[t % 2][:, g * 4 * VW:(g + 1) * 4 * VW],
                                            ot[:, k, g, t * P:(t + 1) * P], ident[0:4 * VW, 0:4 * VW])
                    last.then_inc(turned[t % 2], 1)

            def main(c, k, i):
                if not project:
                    return
                for s in range(2):
                    pe.wait_ge(pt_read[s], ONE + c * 2 + 2)
                for e in range(EC):
                    pe.wait_ge(a_lo[e], ONE + c)
                    for t in range(TC):
                        last = pe.transpose(pe_t[e][:, t * P:(t + 1) * P], att[:, k, t, e * P:(e + 1) * P],
                                            ident[:, :])
                    last.then_inc(att_turned[e], 1)
                for e in range(EC):
                    pe.wait_ge(a_lo[e], ONE + c + 1)
                for s in range(2):
                    pe.wait_ge(y_read[s], ONE + c)
                    for r in range(2):
                        t = 2 * s + r
                        last = split3(pe, py[s][:, r, :], lambda e: ah[:, e, t * P:(t + 1) * P],
                                      lambda e: al[:, e, t * P:(t + 1) * P], lambda e: wh[:, e, :],
                                      lambda e: wl[:, e, :], range(EC))
                    last.then_inc(y_ready[s], 1)

            chunk_pipeline(pe, front, main)

        @block.scalar
        def _(act):
            if project:
                act.wait_ge(s_w, ONE + 32)
                act.activation(wh[:, :, :], w32[:, :, :], ACT.Copy, scale=WS).then_inc(s_wh, 1)

                def main(c, k, i):
                    after(act, y_ready[1], c)
                    for e in range(EC):
                        act.wait_ge(att_turned[e], ONE + c + 1)
                        act.activation(ah[:, e, :], pe_t[e][:, :], ACT.Copy, scale=AS).then_inc(a_hi[e], 1)

                chunk_pipeline(act, lambda c, k, i: None, main)
            stats.root(act)

        @block.gpsimd
        def _(pool):
            if not project:
                return
            pool.wait_ge(s_w, ONE + 32)

            def front(c, k, i):
                pass

            def main(c, k, i):
                for t in range(TC):
                    pool.tensor_tensor(x_res[:, c * TC + t, :], x_res[:, c * TC + t, :], bp[:, :], ALU.add)\
                        .then_inc(biased, 1)

            chunk_pipeline(pool, front, main)

        @block.vector
        def _(dve):
            if project:
                dve.wait_ge(s_wh, ONE + 1)
                dve.scalar_tensor_tensor(out=wl[:, :, :], in0=w32[:, :, :], scalar=WS, in1=wh[:, :, :],
                                         op0=ALU.mult, op1=ALU.subtract).then_inc(s_wl, 1)

            def front(c, k, i):
                if project:
                    after(dve, att_turned[EC - 1], c - 1)
                else:
                    after(dve, x_done, c - 1)
                for t in range(TC):
                    dve.wait_ge(turned[t % 2], ONE + c * 2 + t // 2 + 1)
                    src = pt[t % 2][:, 0:H * VW].rearrange("p (h w) -> p h w", w=VW)
                    dve.reciprocal(rec[:, t % 2, :], src[:, :, DH]).then_inc(rec_done, 1)
                    dve.wait_ge(rec_done, ONE + c * TC + t + 1)
                    dve.scalar_tensor_tensor(out=att[:, k, t, :].rearrange("p (h w) -> p h w", w=DH),
                                             in0=src[:, :, 0:DH], scalar=1.0,
                                             in1=rec[:, t % 2, :].unsqueeze(2).to_broadcast([P, H, DH]),
                                             op0=ALU.mult, op1=ALU.mult)\
                       .then_inc(pt_read[t % 2], 1)

            def main(c, k, i):
                if project:
                    for e in range(EC):
                        dve.wait_ge(a_hi[e], ONE + c + 1)
                        dve.scalar_tensor_tensor(out=al[:, e, :], in0=pe_t[e][:, :], scalar=AS,
                                                 in1=ah[:, e, :], op0=ALU.mult, op1=ALU.subtract)\
                           .then_inc(a_lo[e], 1)
                    dve.wait_ge(biased, ONE + c * TC + TC)
                    for s in range(2):
                        dve.wait_ge(y_ready[s], ONE + c + 1)
                        xs = x_res[:, bass.ds(c * TC + 2 * s, 2), :]
                        dve.scalar_tensor_tensor(out=xs, in0=py[s][:, :, :], scalar=1.0 / (AS * WS), in1=xs,
                                                 op0=ALU.mult, op1=ALU.add).then_inc(y_read[s], 1)
                    for s in range(2):
                        dve.wait_ge(y_read[s], ONE + c + 1)
                else:
                    for s in range(2):
                        dve.wait_ge(pt_read[s], ONE + c * 2 + 2)
                    xs = x_res[:, bass.ds(c * TC, TC), :]
                    dve.tensor_tensor(xs, xs, att[:, k, :, :], ALU.add).then_inc(x_done, 1)
                    dve.wait_ge(x_done, ONE + c + 1)
                for t in range(TC):
                    stats.tile(dve, x_res, c * TC + t)

            chunk_pipeline(dve, front, main)
            stats.finish(dve)


def stage_gate(nc, tag, x_res, mean, rstd, ident, xh, xl, gate_in, comb):
    with ExitStack() as ctx:
        def sb(n, shape, dt):
            return ctx.enter_context(nc.sbuf_tensor(f"{tag}_{n}", shape, dt))

        sem = Semaphores(nc, ctx, tag)

        g32 = sb("g32", [P, EC, E], F32)
        gh, gl = sb("gh", [P, EC, E], F16), sb("gl", [P, EC, E], F16)
        iota = sb("iota", [P, E], F32)
        logit = sb("logit", [P, 2, TC, E], F32)
        spare = sb("spare", [P, 2], F32)
        top_c = sb("top_c", [P, 2, TC, 8], F32)
        pos_c = sb("pos_c", [P, 2, TC, 8], U32)
        top = sb("top", [P, NT, 8], F32)
        posf = sb("posf", [P, NT, 8], F32)
        dif, th = sb("dif", [P, NT], F32), sb("th", [P, NT], F32)
        w1, w2 = sb("w1", [P, NT], F32), sb("w2", [P, NT], F32)
        c2 = sb("c2", [P, NT, E], F32)
        pg_bank = [ctx.enter_context(nc.psum_tensor(f"{tag}_pg{s}", [P, CH], F32)) for s in range(2)]
        pg = [b[:, 0:TC * E].rearrange("p (t e) -> p t e", e=E) for b in pg_bank]
        fr = Front(nc, ctx, sem, tag, x_res, mean, rstd, ident,
                   lambda c, k: xh[:, :, bass.ds(c * CH, CH)], lambda c, k: xl[:, :, bass.ds(c * CH, CH)])
        s_w, s_wh, s_wl, s_iota = sem("w"), sem("whi"), sem("wlo"), sem("iota_ready")
        g_ready = [sem(f"g_ready{k}") for k in range(2)]
        g_copied = [sem(f"g_copied{k}") for k in range(2)]
        s_top, s_kept, s_th, s_fin = sem("top_done"), sem("kept"), sem("th_done"), sem("fin")
        sem.start()
        block = ctx.enter_context(nc.Block())

        @block.sync
        def _(sp):
            sp.dma_start(g32[:, :, :], gate_in).then_inc(s_w, 16)

        @block.gpsimd
        def _(pool):
            pool.iota(iota[:, :], pattern=[[1, E]], base=0, channel_multiplier=0,
                      allow_small_or_imprecise_dtypes=True).then_inc(s_iota, 1)

        @block.scalar
        def _(act):
            act.wait_ge(s_w, ONE + 16)
            act.activation(gh[:, :, :], g32[:, :, :], ACT.Copy, scale=WS).then_inc(s_wh, 1)
            chunk_pipeline(act, lambda c, k, i: fr.hi(act, c, k, i), lambda c, k, i: None)
            act.wait_ge(s_fin, ONE + 1)
            act.activation(th[:, :], dif[:, :], ACT.Tanh, scale=0.5).then_inc(s_th, 1)

        @block.tensor
        def _(pe):
            pe.wait_ge(s_wl, ONE + 1)

            def main(c, k, i):
                fr.split_ready(pe, c)
                pe.wait_ge(g_copied[k], ONE + i)
                for t in range(TC):
                    tok = c * CH + t * P
                    last = split3(pe, pg[k][:, t, :], lambda e: xh[:, e, bass.ds(tok, P)],
                                  lambda e: xl[:, e, bass.ds(tok, P)], lambda e: gh[:, e, :],
                                  lambda e: gl[:, e, :], range(EC))
                last.then_inc(g_ready[k], 1)

            chunk_pipeline(pe, lambda c, k, i: fr.transpose(pe, c, k, i), main)

        @block.vector
        def _(dve):
            dve.wait_ge(s_wh, ONE + 1)
            dve.scalar_tensor_tensor(out=gl[:, :, :], in0=g32[:, :, :], scalar=WS, in1=gh[:, :, :],
                                     op0=ALU.mult, op1=ALU.subtract).then_inc(s_wl, 1)

            def front(c, k, i):
                fr.lo(dve, c, k, i)
                fr.norm_next(dve, c, k, i)

            def main(c, k, i):
                dve.wait_ge(g_ready[k], ONE + i + 1)
                dve.tensor_scalar(logit[:, k, :, :], pg[k][:, :, :], PS, None, ALU.mult).then_inc(g_copied[k], 1)
                dve.wait_ge(g_copied[k], ONE + i + 1)
                dve.memset(spare[:, 0:1], 0.0)
                for t in range(TC):
                    dve.max(top_c[:, k, t, :], logit[:, k, t, :]).then_inc(s_top, 1)
                dve.wait_ge(s_top, ONE + c * (2 * TC) + TC)
                dve.memset(spare[:, 1:2], 0.0)
                for t in range(TC):
                    dve.max_index(pos_c[:, k, t, :], top_c[:, k, t, :], logit[:, k, t, :]).then_inc(s_top, 1)
                dve.wait_ge(s_top, ONE + c * (2 * TC) + 2 * TC)
                dve.tensor_copy(top[:, bass.ds(c * TC, TC), :], top_c[:, k, :, :]).then_inc(s_kept, 1)
                dve.tensor_copy(posf[:, bass.ds(c * TC, TC), :], pos_c[:, k, :, :]).then_inc(s_kept, 1)

            fr.norm(dve, 0, 0, 0)
            chunk_pipeline(dve, front, main)
            dve.wait_ge(s_kept, ONE + 2 * NC)
            dve.tensor_tensor(dif[:, :], top[:, :, 0], top[:, :, 1], ALU.subtract).then_inc(s_fin, 1)
            dve.wait_ge(s_th, ONE + 1)
            dve.tensor_scalar(w1[:, :], th[:, :], 0.5 * YS, 0.5 * YS, ALU.mult, ALU.add).then_inc(s_fin, 1)
            dve.tensor_scalar(w2[:, :], th[:, :], -0.5 * YS, 0.5 * YS, ALU.mult, ALU.add).then_inc(s_fin, 1)
            dve.wait_ge(s_iota, ONE + 1)
            dve.wait_ge(s_fin, ONE + 3)
            for n, (dst, w) in enumerate(((comb, w1), (c2, w2))):
                dve.tensor_tensor(dst[:, :, 0:E], iota[:, :].unsqueeze(1).to_broadcast([P, NT, E]),
                                  posf[:, :, n:n + 1].to_broadcast([P, NT, E]), ALU.is_equal).then_inc(s_fin, 1)
                dve.wait_ge(s_fin, ONE + 4 + 2 * n)
                dve.tensor_tensor(dst[:, :, 0:E], dst[:, :, 0:E], w[:, :].unsqueeze(2).to_broadcast([P, NT, E]),
                                  ALU.mult).then_inc(s_fin, 1)
                dve.wait_ge(s_fin, ONE + 5 + 2 * n)
            dve.memset(comb[:, :, E:E + 1], YS).then_inc(s_fin, 1)
            dve.tensor_tensor(comb[:, :, 0:E], comb[:, :, 0:E], c2[:, :, :], ALU.add).then_inc(s_fin, 1)
            dve.wait_ge(s_fin, ONE + 9)


def stage_experts(nc, tag, x_res, xh, xl, comb, up_in, down_in, x_dram):
    with ExitStack() as ctx:
        def sb(n, shape, dt):
            return ctx.enter_context(nc.sbuf_tensor(f"{tag}_{n}", shape, dt))

        sem = Semaphores(nc, ctx, tag)

        u32 = sb("u32", [P, EC, 2 * F], F32)
        d32 = sb("d32", [P, FC, D], F32)
        uh = [sb(f"uh{s}", [P, EC, 2 * F], F16) for s in range(2)]
        ul = [sb(f"ul{s}", [P, EC, 2 * F], F16) for s in range(2)]
        dh = [sb(f"dh{s}", [P, FC, D], F16) for s in range(2)]
        dl = [sb(f"dl{s}", [P, FC, D], F16) for s in range(2)]
        gate = [sb(f"gate{s}", [P, CH], F32) for s in range(2)]
        hid = [sb(f"hid{s}", [P, CH], F32) for s in range(2)]
        hh = [sb(f"hh{k}", [P, FC, CH], F16) for k in range(2)]
        hl = [sb(f"hl{k}", [P, FC, CH], F16) for k in range(2)]
        pg = [ctx.enter_context(nc.psum_tensor(f"{tag}_pg{s}", [P, CH], F32)) for s in range(2)]
        pu = [ctx.enter_context(nc.psum_tensor(f"{tag}_pu{s}", [P, CH], F32)) for s in range(2)]
        py = [ctx.enter_context(nc.psum_tensor(f"{tag}_py{s}", [P, 2, D], F32)) for s in range(2)]
        w_loaded, w_hi, w_lo = sem("w_loaded"), sem("w_hi"), sem("w_lo")
        gu_ready = [sem(f"gu_ready{s}") for s in range(2)]
        gate_done = [sem(f"gate_done{s}") for s in range(2)]
        hid_done = [sem(f"hid_done{s}") for s in range(2)]
        hid_hi = [sem(f"hid_hi{s}") for s in range(2)]
        hid_lo = [sem(f"hid_lo{s}") for s in range(2)]
        y_ready = [[sem(f"y_ready{k}{m}") for m in range(2)] for k in range(2)]
        y_added = [sem(f"y_added{s}") for s in range(2)]
        x_stored = sem("x_stored")
        sem.start()
        block = ctx.enter_context(nc.Block())

        def experts(eng, prepare, front, main):
            def one(e, s):
                chunk_pipeline(eng, lambda c, k, i: front(e, s, c, k, i), lambda c, k, i: main(e, s, c, k, i))
            prepare(0, 0)
            with eng.Fori(0, E // 2) as pair:
                prepare(pair * 2 + 1, 1)
                one(pair * 2, 0)
                prepare(pair * 2 + 2, 0)
                one(pair * 2 + 1, 1)
            one(E, 0)

        def slot(f, e, k, i):
            n = FC * k + f
            return n % 2, e * (NC * FC // 2) + i * FC + n // 2

        @block.sync
        def _(sp):
            def prepare(e, s):
                after(sp, w_lo, e * 2)
                sp.dma_start(u32[:, :, :], up_in[e]).then_inc(w_loaded, 16)
                sp.dma_start(d32[:, :, :], down_in[e]).then_inc(w_loaded, 16)

            prepare(0, 0)
            with sp.Fori(1, E + 1) as e:
                sp.wait_ge(w_lo, ONE + e * 2)
                sp.dma_start(u32[:, :, :], up_in[bass.ds(e, 1)].rearrange("e p a f -> p (e a) f")).then_inc(w_loaded, 16)
                sp.dma_start(d32[:, :, :], down_in[bass.ds(e, 1)].rearrange("e p a f -> p (e a) f")).then_inc(w_loaded, 16)
            with sp.Fori(0, NC) as c:
                for s in range(2):
                    sp.wait_ge(y_added[s], ONE + c + E * NC + 1)
                sp.dma_start(x_dram[bass.ds(c * CH, CH), :].rearrange("(t p) d -> p t d", p=P),
                             x_res[:, bass.ds(c * TC, TC), :]).then_inc(x_stored, 16)
            sp.wait_ge(x_stored, ONE + NC * 16)

        @block.scalar
        def _(act):
            def prepare(e, s):
                act.wait_ge(w_loaded, ONE + e * 32 + 32)
                after(act, y_ready[1][1], (e - 1) * (NC // 2))
                act.activation(uh[s][:, :, :], u32[:, :, :], ACT.Copy, scale=WS).then_inc(w_hi, 1)
                act.activation(dh[s][:, :, :], d32[:, :, :], ACT.Copy, scale=WS).then_inc(w_hi, 1)

            def front(e, s, c, k, i):
                for f in range(FC):
                    b, use = slot(f, e, k, i)
                    act.wait_ge(gu_ready[b], ONE + use + 1)
                    act.wait_ge(hid_done[b], ONE + use)
                    act.activation(gate[b][:, :], pg[b][:, :], ACT.Silu, scale=PS).then_inc(gate_done[b], 1)

            experts(act, prepare, front, lambda e, s, c, k, i: None)

        @block.gpsimd
        def _(pool):
            def prepare(e, s):
                pass

            def front(e, s, c, k, i):
                for f in range(FC):
                    b, use = slot(f, e, k, i)
                    pool.wait_ge(hid_hi[b], ONE + use + 1)
                    pool.tensor_tensor(hl[k][:, f, :], hid[b][:, :], hh[k][:, f, :], ALU.subtract)\
                        .then_inc(hid_lo[b], 1)

            experts(pool, prepare, front, lambda e, s, c, k, i: None)

        @block.vector
        def _(dve):
            def prepare(e, s):
                dve.wait_ge(w_hi, ONE + e * 2 + 2)
                dve.scalar_tensor_tensor(out=ul[s][:, :, :], in0=u32[:, :, :], scalar=WS, in1=uh[s][:, :, :],
                                         op0=ALU.mult, op1=ALU.subtract).then_inc(w_lo, 1)
                dve.scalar_tensor_tensor(out=dl[s][:, :, :], in0=d32[:, :, :], scalar=WS, in1=dh[s][:, :, :],
                                         op0=ALU.mult, op1=ALU.subtract).then_inc(w_lo, 1)

            def front(e, s, c, k, i):
                dve.wait_ge(y_ready[k][1], ONE + e * (NC // 2) + i)
                for f in range(FC):
                    b, use = slot(f, e, k, i)
                    dve.wait_ge(gate_done[b], ONE + use + 1)
                    dve.wait_ge(hid_lo[b], ONE + use)
                    dve.scalar_tensor_tensor(out=hid[b][:, :], in0=pu[b][:, :], scalar=PS * HS,
                                             in1=gate[b][:, :], op0=ALU.mult, op1=ALU.mult)\
                       .then_inc(hid_done[b], 1)
                    dve.wait_ge(hid_done[b], ONE + use + 1)
                    dve.tensor_copy(hh[k][:, f, :], hid[b][:, :]).then_inc(hid_hi[b], 1)

            def main(e, s, c, k, i):
                for m in range(2):
                    dve.wait_ge(y_ready[k][m], ONE + e * (NC // 2) + i + 1)
                    for r in range(2):
                        ti = c * TC + (2 * m + r)
                        xs = x_res[:, ti, :]
                        last = dve.scalar_tensor_tensor(out=xs, in0=py[m][:, r, :], scalar=comb[:, ti, e:e + 1] if isinstance(e, int)
                                                        else comb[:, bass.ds(ti, 1), bass.ds(e, 1)].rearrange("p a b -> p (a b)"),
                                                        in1=xs, op0=ALU.mult, op1=ALU.add)
                    last.then_inc(y_added[m], 1)

            experts(dve, prepare, front, main)

        @block.tensor
        def _(pe):
            def prepare(e, s):
                pass

            def front(e, s, c, k, i):
                if k == 0:
                    pe.wait_ge(w_lo, ONE + e * 2 + 2)
                for f in range(FC):
                    b, use = slot(f, e, k, i)
                    pe.wait_ge(hid_done[b], ONE + use)
                    for dst, f0 in ((pg[b], f * P), (pu[b], F + f * P)):
                        last = split3(pe, dst[:, :], lambda a: uh[s][:, a, f0:f0 + P],
                                      lambda a: ul[s][:, a, f0:f0 + P],
                                      lambda a: xh[:, a, bass.ds(c * CH, CH)],
                                      lambda a: xl[:, a, bass.ds(c * CH, CH)], range(EC))
                    last.then_inc(gu_ready[b], 1)

            def main(e, s, c, k, i):
                for f in range(FC):
                    b, use = slot(f, e, k, i)
                    pe.wait_ge(hid_lo[b], ONE + use + 1)
                for m in range(2):
                    pe.wait_ge(y_added[m], ONE + e * NC + c)
                    for r in range(2):
                        t = 2 * m + r
                        last = split3(pe, py[m][:, r, :], lambda f: hh[k][:, f, t * P:(t + 1) * P],
                                      lambda f: hl[k][:, f, t * P:(t + 1) * P], lambda f: dh[s][:, f, :],
                                      lambda f: dl[s][:, f, :], range(FC))
                    last.then_inc(y_ready[k][m], 1)

            experts(pe, prepare, front, main)


def stage_ternary(nc, tag, x_res, mean, rstd, ident, w_in, alpha_in, bias_in, out):
    with ExitStack() as ctx:
        def sb(n, shape, dt):
            return ctx.enter_context(nc.sbuf_tensor(f"{tag}_{n}", shape, dt))

        sem = Semaphores(nc, ctx, tag)

        w = sb("w", [P, EC, D], F32)
        neg, mag, above = sb("neg", [P, EC, D], F32), sb("mag", [P, EC, D], F32), sb("above", [P, EC, D], F32)
        tern = sb("tern", [P, EC, D], F16)
        part, thr = sb("part", [P, 1], F32), sb("thr", [P, 2], F32)
        ones = sb("ones", [P, P], F32)
        bias = sb("bias", [P, D], F32)
        alpha, alpha_s = sb("alpha", [P, 1], F32), sb("alpha_s", [P, 1], F32)
        xh, xl = sb("xh", [P, 2, EC, CH], F16), sb("xl", [P, 2, EC, CH], F16)
        py = [ctx.enter_context(nc.psum_tensor(f"{tag}_py{s}", [P, 2, D], F32)) for s in range(2)]
        psum_abs = ctx.enter_context(nc.psum_tensor(f"{tag}_pabs", [P, CH], F32))
        fr = Front(nc, ctx, sem, tag, x_res, mean, rstd, ident, lambda c, k: xh[:, k], lambda c, k: xl[:, k])
        s_w, prep, s_sum = sem("w_loaded"), sem("prep"), sem("abs_sum")
        biased = sem("biased")
        y_ready = [sem(f"y_ready{s}") for s in range(2)]
        y_added = [sem(f"y_added{s}") for s in range(2)]
        stored = sem("stored")
        sem.start()
        block = ctx.enter_context(nc.Block())

        @block.sync
        def _(sp):
            sp.dma_start(w[:, :, :], w_in).then_inc(s_w, 16)
            sp.dma_start(bias[:, :], bias_in.partition_broadcast(P)).then_inc(s_w, 16)
            sp.dma_start(alpha[:, :], alpha_in.partition_broadcast(P)).then_inc(s_w, 16)

            with sp.Fori(0, B) as b:
                for m in range(2):
                    sp.wait_ge(y_added[m], ONE + b * 2 + 1)
                sp.dma_start(out[bass.ds(b * N, 64), :], x_res[0:64, b * TB, :]).then_inc(stored, 16)
                sp.dma_start(out[bass.ds(b * N + (N - 64), 64), :], x_res[64:128, b * TB, :]).then_inc(stored, 16)
                sp.dma_start(out[bass.ds(b * N + 64, 3 * P), :].rearrange("(t p) d -> p t d", p=P),
                             x_res[:, bass.ds(b * TB + 1, 3), :]).then_inc(stored, 16)
                for m in range(2):
                    sp.wait_ge(y_added[m], ONE + b * 2 + 2)
                sp.dma_start(out[bass.ds(b * N + (64 + 3 * P), 4 * P), :].rearrange("(t p) d -> p t d", p=P),
                             x_res[:, bass.ds(b * TB + 4, 4), :]).then_inc(stored, 16)
            sp.wait_ge(stored, ONE + B * 64)

        @block.gpsimd
        def _(pool):
            pool.wait_ge(s_w, ONE + 48)

            def main(c, k, i):
                pool.wait_ge(fr.normed[k], ONE + i * TC + TC)
                for t in range(TC):
                    ti = c * TC + t
                    pool.tensor_tensor(x_res[:, ti, :], x_res[:, ti, :], bias[:, :], ALU.add).then_inc(biased, 1)

            chunk_pipeline(pool, lambda c, k, i: None, main)

        @block.scalar
        def _(act):
            def front(c, k, i):
                after(act, y_ready[1], c - 1)
                fr.hi(act, c, k, i)

            chunk_pipeline(act, front, lambda c, k, i: None)

        @block.vector
        def _(dve):
            dve.memset(ones[:, :], 1.0).then_inc(prep, 1)
            dve.wait_ge(s_w, ONE + 48)
            dve.tensor_scalar(neg[:, :, :], w[:, :, :], -1.0, None, ALU.mult).then_inc(prep, 1)
            dve.wait_ge(prep, ONE + 2)
            dve.tensor_tensor(mag[:, :, :], w[:, :, :], neg[:, :, :], ALU.max).then_inc(prep, 1)
            dve.wait_ge(prep, ONE + 3)
            dve.tensor_reduce(part[:, :], mag[:, :, :].rearrange("p e f -> p (e f)"), AXX, ALU.add).then_inc(prep, 1)
            dve.tensor_scalar(alpha_s[:, :], alpha[:, :], 1.0 / XS, None, ALU.mult).then_inc(prep, 1)
            dve.wait_ge(s_sum, ONE + 1)
            dve.tensor_scalar(thr[:, 0:1], psum_abs[:, 0:1], 0.7 / (D * D), None, ALU.mult).then_inc(prep, 1)
            dve.tensor_scalar(thr[:, 1:2], psum_abs[:, 0:1], -0.7 / (D * D), None, ALU.mult).then_inc(prep, 1)
            dve.wait_ge(prep, ONE + 7)
            dve.tensor_scalar(above[:, :, :], w[:, :, :], thr[:, 0:1], None, ALU.is_gt).then_inc(prep, 1)
            dve.tensor_scalar(neg[:, :, :], w[:, :, :], thr[:, 1:2], None, ALU.is_lt).then_inc(prep, 1)
            dve.wait_ge(prep, ONE + 9)
            dve.tensor_tensor(tern[:, :, :], above[:, :, :], neg[:, :, :], ALU.subtract).then_inc(prep, 1)

            def front(c, k, i):
                after(dve, y_ready[1], c - 1)
                fr.lo(dve, c, k, i)
                fr.norm_next(dve, c, k, i)

            def main(c, k, i):
                dve.wait_ge(biased, ONE + c * TC + TC)
                for m in range(2):
                    dve.wait_ge(y_ready[m], ONE + c + 1)
                    xs = x_res[:, bass.ds(c * TC + 2 * m, 2), :]
                    dve.scalar_tensor_tensor(out=xs, in0=py[m][:, :, :], scalar=alpha_s[:, 0:1], in1=xs,
                                             op0=ALU.mult, op1=ALU.add).then_inc(y_added[m], 1)

            fr.norm(dve, 0, 0, 0)
            chunk_pipeline(dve, front, main)

        @block.tensor
        def _(pe):
            pe.wait_ge(prep, ONE + 4)
            pe.matmul(psum_abs[:, 0:1], ones[:, :], part[:, :], start=True, stop=True).then_inc(s_sum, 1)
            pe.wait_ge(prep, ONE + 10)

            def main(c, k, i):
                fr.split_ready(pe, c)
                for m in range(2):
                    pe.wait_ge(y_added[m], ONE + c)
                    for r in range(2):
                        t = 2 * m + r
                        for n, (part_x, e) in enumerate([(x, e) for x in (xh, xl) for e in range(EC)]):
                            last = pe.matmul(py[m][:, r, :], part_x[:, k, e, t * P:(t + 1) * P], tern[:, e, :],
                                             start=(n == 0), stop=(n == 2 * EC - 1))
                    last.then_inc(y_ready[m], 1)

            chunk_pipeline(pe, lambda c, k, i: fr.transpose(pe, c, k, i), main)


def stage_constants(nc, ident, ident16, identb, wmask, zrow, mrow, qx, kx):
    with ExitStack() as ctx:
        sem = Semaphores(nc, ctx, "c")
        s_set, s_cut, s_row = sem("set"), sem("cut"), sem("row")
        sem.start()
        block = ctx.enter_context(nc.Block())

        @block.vector
        def _(dve):
            for m in (ident, ident16, identb):
                dve.memset(m[:, :], 0.0).then_inc(s_set, 1)
            dve.memset(wmask[:, :, :], 0.0).then_inc(s_set, 1)
            dve.memset(zrow[:, :], 0.0).then_inc(s_set, 1)
            dve.memset(mrow[:, :], MROW).then_inc(s_set, 1)

        @block.gpsimd
        def _(pool):
            pool.wait_ge(s_set, ONE + 6)
            for m in (ident, ident16, identb):
                pool.affine_select(out=m[:, :], in_=m[:, :], compare_op=ALU.not_equal, fill=1.0, base=0,
                                   pattern=[[-1, P]], channel_multiplier=1).then_inc(s_cut, 1)
            pool.affine_select(out=wmask[:, 0, :], in_=wmask[:, 0, :], compare_op=ALU.is_ge, fill=NEG, base=0,
                               pattern=[[1, P]], channel_multiplier=-1).then_inc(s_cut, 1)
            pool.affine_select(out=wmask[:, 1, :], in_=wmask[:, 1, :], compare_op=ALU.is_ge, fill=NEG, base=0,
                               pattern=[[-1, P]], channel_multiplier=1).then_inc(s_cut, 1)
            pool.wait_ge(s_cut, ONE + 5)

        @block.sync
        def _(sp):
            sp.wait_ge(s_set, ONE + 6)
            for x, row in ((qx, zrow), (kx, mrow)):
                for g in range(2 * HG):
                    sp.dma_start(x[g, TR - 1, :, :].rearrange("i (a n) -> (i a) n", n=N), row[:, :]).then_inc(s_row, 16)
            sp.wait_ge(s_row, ONE + 4 * HG * 16)


def build(nc, x, l0_wqkv, l0_bqk, l0_bv, l0_wp, l0_bp, gate_w, up_w, down_w, l1_wqkv, l1_bqk, l1_bv,
          tern_w, tern_alpha, tern_bias, brows, out):
    qx = nc.dram_tensor("qx", [2 * HG, TR, 2, T], F16, kind="Internal").ap()
    kx = nc.dram_tensor("kx", [2 * HG, TR, 2, T], F16, kind="Internal").ap()
    vx = nc.dram_tensor("vx", [T, H * VW], F32, kind="Internal").ap()
    ox = nc.dram_tensor("ox", [HG, 4 * VW, T], F32, kind="Internal").ap()
    x2 = nc.dram_tensor("x2", [T, D], F32, kind="Internal").ap()
    with ExitStack() as ctx:
        def sb(n, shape, dt):
            return ctx.enter_context(nc.sbuf_tensor(n, shape, dt))
        ident, ident16, identb = sb("ident", [P, P], F32), sb("ident16", [P, P], F16), sb("identb", [P, P], BF16)
        wmask = sb("wmask", [P, 2, P], BF16)
        mean, rstd = sb("mean", [P, NT], F32), sb("rstd", [P, NT], F32)
        with ExitStack() as rows:
            zrow = rows.enter_context(nc.sbuf_tensor("zrow", [2 * B, N], F16))
            mrow = rows.enter_context(nc.sbuf_tensor("mrow", [2 * B, N], F16))
            stage_constants(nc, ident, ident16, identb, wmask, zrow, mrow, qx, kx)
        x_res = sb("x_res", [P, NT, D], F32)
        stage_stats(nc, "n0", x, x_res, mean, rstd, False)
        stage_project(nc, "p0", x_res, mean, rstd, ident, l0_wqkv, (l0_bqk, l0_bv), qx, kx, vx)
        stage_attend(nc, "a0", window_jobs(), 1.0 / (QS * QS * D ** 0.5), identb, wmask, None, ident16, qx, kx, vx, ox)
        stage_combine(nc, "c0", x_res, mean, rstd, ident, ox, l0_wp, l0_bp)
        with ExitStack() as moe:
            xh = moe.enter_context(nc.sbuf_tensor("xh", [P, EC, T], F16))
            xl = moe.enter_context(nc.sbuf_tensor("xl", [P, EC, T], F16))
            comb = moe.enter_context(nc.sbuf_tensor("comb", [P, NT, E + 1], F32))
            stage_gate(nc, "g", x_res, mean, rstd, ident, xh, xl, gate_w, comb)
            stage_experts(nc, "e", x_res, xh, xl, comb, up_w, down_w, x2)
        stage_stats(nc, "n1", x2, x_res, mean, rstd, True)
        stage_project(nc, "p1", x_res, mean, rstd, ident, l1_wqkv, (l1_bqk, l1_bv), qx, kx, vx)
        stage_attend(nc, "a1", block_jobs(), 1.0 / (QS * QS * DH ** 0.5), identb, None, brows, ident16, qx, kx, vx, ox)
        stage_combine(nc, "c1", x_res, mean, rstd, ident, ox, None, None)
        stage_ternary(nc, "t", x_res, mean, rstd, ident, tern_w, tern_alpha, tern_bias, out)


def kernel(**inputs):
    import concourse.bacc as bacc
    from concourse.bass_utils import run_bass_kernel_spmd

    a = {k: np.asarray(v) for k, v in inputs.items()}
    order = np.arange(D).reshape(HG, 2, 2, DH).transpose(0, 2, 3, 1).reshape(D)

    def cols(w):
        return w.T.reshape(-1, P, w.shape[0]).transpose(1, 0, 2)

    def qkv(layer):
        wq, wk, wv = (a[f"{layer}_W{n}"] for n in "qkv")
        w = np.stack([cols(wq[order]), cols(wk[order]), cols(wv)], axis=1)
        b = np.stack([a[f"{layer}_bq"][order].reshape(2, P), a[f"{layer}_bk"][order].reshape(2, P)])
        return w, b.reshape(4, P).T, a[f"{layer}_bv"]

    up = np.stack([cols(w) for w in a["L0_ffn_w_up"]]
                  + [np.concatenate([cols(a["L0_ffn_sg_gate"]), cols(a["L0_ffn_sg_up"])], axis=2)])
    down = np.stack([cols(w) for w in a["L0_ffn_w_down"]] + [cols(a["L0_ffn_sg_down"])])
    w0, bqk0, bv0 = qkv("L0_attn")
    w1, bqk1, bv1 = qkv("L1_attn")
    arrays = {
        "x": a["L0_attn_x"].reshape(T, D), "l0_wqkv": w0, "l0_bqk": bqk0, "l0_bv": bv0,
        "l0_wp": cols(a["L0_attn_Wp"]), "l0_bp": a["L0_attn_bp"], "gate_w": cols(a["L0_ffn_gate_w"]),
        "up_w": up, "down_w": down, "l1_wqkv": w1, "l1_bqk": bqk1, "l1_bv": bv1,
        "tern_w": cols(a["L1_ffn_weight"]), "tern_alpha": a["L1_ffn_alpha"], "tern_bias": a["L1_ffn_bias"],
        "brows": block_rows(),
    }
    arrays = {k: np.ascontiguousarray(v) for k, v in arrays.items()}
    nc = bacc.Bacc("TRN2", target_bir_lowering=False, num_devices=1)
    args = [nc.dram_tensor(k, v.shape, mybir.dt.from_np(v.dtype), kind="ExternalInput").ap()
            for k, v in arrays.items()]
    out = nc.dram_tensor("out", [T, D], F32, kind="ExternalOutput").ap()
    build(nc, *args, out)
    r = run_bass_kernel_spmd(nc, [arrays], core_ids=[0])
    return r.results[0]["out"].reshape(B, N, D)
```
